# Optimizing a Trainium2 kernel written in Bass

```python
import numpy as np
import jax
import jax.numpy as jnp

def _softmax(x, axis=-1):
    return jax.nn.softmax(x, axis=axis)

def _gelu(x):
    return jax.nn.gelu(x, approximate=True)

def _silu(x):
    return jax.nn.silu(x)

def _sigmoid(x):
    return jax.nn.sigmoid(x)

def _layernorm(x, axis=-1, eps=1e-05):
    m = jnp.mean(x, axis=axis, keepdims=True)
    v = jnp.var(x, axis=axis, keepdims=True)
    return (x - m) / jnp.sqrt(v + eps)

def _scatter_add(tgt, idx, src, axis=0):
    return tgt.at[idx].add(src)

def _segment_sum(src, seg, n):
    return jax.ops.segment_sum(src, seg, n)
kernel_name = 'mk_adj_preln_d1_adj_r2_12e606'

def setup_inputs(seed: int=0):
    np.random.seed(seed)
    _w = jnp.asarray

    def _rec_inputs():
        import jax
        import jax.numpy as jnp
        _gk = jax.random.key(seed)
        x = -0.0002928 + 1 * jax.random.normal(jax.random.fold_in(_gk, 1), (4096, 256), jnp.float32)
        _w = (1.0 + jnp.arange(4096, dtype=jnp.float32)) ** (-0.5)
        _w = _w / _w.mean()
        _pij = jnp.clip(0.00195312 * _w[:, None] * _w[None, :], 0.0, 1.0)
        _a = jax.random.uniform(jax.random.fold_in(_gk, 2), (4096, 4096)) < _pij
        _af = _a.astype(jnp.float32)
        adj = _af
        return (x, adj)
    x, adj = _rec_inputs()

    def _L0_gnn_setup():
        import jax, jax.numpy as jnp
        import numpy as np
        SIZE_U = 2048
        SIZE_V = 2048
        N = SIZE_U + SIZE_V
        C_IN = 256
        C_OUT = 256
        EDGE_P = 0.005
        LEAKY_SLOPE = 0.01

        def _xavier_uniform(key, shape):
            fan_in, fan_out = shape
            lim = float(np.sqrt(6.0 / (fan_in + fan_out)))
            return jax.random.uniform(key, shape, jnp.float32, minval=-lim, maxval=lim)
        key = jax.random.key(seed)
        k1, k2, k3, k4 = jax.random.split(key, 4)
        x = jax.random.normal(k1, (N, C_IN), jnp.float32)
        adj = (jax.random.uniform(k2, (N, N)) < EDGE_P).astype(jnp.float32)
        weightr = _xavier_uniform(k3, (C_IN, C_OUT))
        weightd = _xavier_uniform(k4, (C_IN, C_OUT))
        bias = jnp.zeros((C_OUT,), jnp.float32)
        return {'x': x, 'adj': adj, 'weightr': weightr, 'weightd': weightd, 'bias': bias}
    _L0_gnn_all = _L0_gnn_setup()
    _L0_gnn_in = {k: v for k, v in _L0_gnn_all.items() if k in ('weightr', 'weightd', 'bias')}
    del _L0_gnn_all
    return {'x': x, 'adj': adj, 'L0_gnn_weightr': _L0_gnn_in['weightr'], 'L0_gnn_weightd': _L0_gnn_in['weightd'], 'L0_gnn_bias': _L0_gnn_in['bias']}

def reference(x, adj, L0_gnn_weightr, L0_gnn_weightd, L0_gnn_bias):
    import jax
    import jax.numpy as jnp

    def _L0_gnn_ref(x, adj, weightr, weightd, bias):
        import jax, jax.numpy as jnp
        import numpy as np
        SIZE_U = 2048
        SIZE_V = 2048
        N = SIZE_U + SIZE_V
        C_IN = 256
        C_OUT = 256
        EDGE_P = 0.005
        LEAKY_SLOPE = 0.01

        def _xavier_uniform(key, shape):
            fan_in, fan_out = shape
            lim = float(np.sqrt(6.0 / (fan_in + fan_out)))
            return jax.random.uniform(key, shape, jnp.float32, minval=-lim, maxval=lim)
        A = adj + jnp.eye(N, dtype=adj.dtype)
        deg = A.sum(axis=1)
        dinv = jnp.where(deg > 0, jax.lax.rsqrt(deg), 0.0)
        A = A * dinv[:, None] * dinv[None, :]
        R = x[:SIZE_U] @ weightr
        D = x[SIZE_U:] @ weightd
        h = jnp.concatenate([R, D], axis=0)
        out = A @ h + bias
        return jax.nn.leaky_relu(out, negative_slope=LEAKY_SLOPE)
    h = jnp.maximum(_layernorm(x, axis=-1), 0.0)
    x = x + _L0_gnn_ref(h, adj, L0_gnn_weightr, L0_gnn_weightd, L0_gnn_bias)
    return x

_drawn_inputs = setup_inputs


def setup_inputs(seed=0):
    import zlib

    import numpy as np

    out = dict(_drawn_inputs(seed))
    spreads = {'L0_gnn_bias': (0.0, 0.1)}
    factors = {}
    for name, (base, spread) in spreads.items():
        noise = np.random.default_rng([zlib.crc32(name.encode()), seed]).standard_normal(out[name].shape)
        drawn = base * np.exp(spread * noise) if base else spread * noise
        out[name] = jnp.asarray(drawn.astype(out[name].dtype))
    for name, factor in factors.items():
        out[name] = (out[name] * factor).astype(out[name].dtype)
    return out
```

```python
from contextlib import ExitStack

import concourse.bass as bass
from concourse import mybir

F32 = mybir.dt.float32
F16 = mybir.dt.float16
F8 = mybir.dt.float8e4
U32 = mybir.dt.uint32
I32 = mybir.dt.int32
U8 = mybir.dt.uint8
ALU = mybir.AluOpType
ACT = mybir.ActivationFunctionType
AX_X = mybir.AxisListType.X
RMAX = bass.bass_isa.ReduceOp.max

P = 128
LANES = 4
EPS = 1e-5
SLOPE = 0.01
DEG_FLOOR = 2.0 ** -100
EXP_MASK = 0x7F800000
RING = 6
HALVES = 2
STAGES = 4


def plan_products(tiles):
    quads, pairs = tiles // LANES, tiles // 2
    load_us, block_us = 5.8, 0.216
    todo = {p: list(range(p // 2, quads)) for p in range(pairs)}
    slots, clock = [], 0.0
    for t in range(tiles + 2):
        items = []
        clock = max(clock, load_us * t) + 0.5
        if 1 <= t <= quads:
            items += [("X", t - 1, 0), ("X", t - 1, 1)]
            clock += 1.0
        if 2 <= t <= quads + 1:
            items += [("H", t - 2, 0), ("H", t - 2, 1)]
            clock += 3.5
        if t % 2 == 1 and t >= 3 and (t - 3) // 4 >= 1:
            p = (t - 3) // 2
            items.append(("M", p, list(range(p // 2))))
            clock += 2 * LANES * len(items[-1][2]) * block_us
        while t < tiles:
            ready = [(len([J for J in js if 4 * J + 6 <= t]), -p) for p, js in todo.items() if 2 * p + 3 <= t]
            ready = [r for r in ready if r[0]]
            if not ready or clock > load_us * (t + 0.8):
                break
            n, p = max(ready)
            js, todo[-p] = todo[-p][:n], todo[-p][n:]
            items.append(("M", -p, js))
            clock += 2 * LANES * n * block_us
        slots.append(items)
    rest = sorted(todo, key=lambda p: -len(todo[p]))
    return slots, [("M", p, todo[p]) for p in rest]


def gnn_layer(nc, x, adj, weightr, weightd, bias, out):
    N, C = x.shape
    TILES = N // P
    QUADS = TILES // LANES
    PAIRS = TILES // 2
    WORDS = N // LANES // P
    KC = C // P
    HALF = N // HALVES
    assert C == 2 * P and WORDS == QUADS and N % (LANES * P) == 0

    x_q = x.rearrange("(q w b) c -> q w b c", w=P, b=LANES)
    out_q = out.rearrange("(q w b) c -> q w b c", w=P, b=LANES)
    adj_q = adj.rearrange("(q w b) m -> q w b m", w=P, b=LANES)

    slots, rest = plan_products(TILES)
    ring_items = [it for s in slots for it in s] + rest
    bank_of, evac_count, seen = [], [], {"act": 0, "dve": 0}
    for n, it in enumerate(ring_items):
        who = "dve" if it[0] == "M" else "act"
        seen[who] += 1
        bank_of.append(n % RING)
        evac_count.append((who, seen[who]))
    sums = [n for n, it in enumerate(ring_items) if it[0] == "M"]
    last_sum = {ring_items[n][1]: k for k, n in enumerate(sums)}
    row_item = {}
    for k, n in enumerate(sums):
        row_item.setdefault(ring_items[n][1], k)

    with ExitStack() as ctx:
        def sb(name, shape, dt):
            return ctx.enter_context(nc.sbuf_tensor(name, shape, dt))

        def sem(name):
            return ctx.enter_context(nc.semaphore(name))

        stage = sb("stage", [P, STAGES, HALF], F32)
        adj8 = sb("adj8", [P, 2, N], F8)
        upper_words = sum(LANES * (QUADS - q) for q in range(QUADS))
        upper = sb("upper", [P, upper_words, P], U32)
        lower = sb("lower", [P, 2, 2, QUADS - 1, P], U32)
        acc = sb("acc", [P, TILES, C], F32)
        gq = sb("gq", [P, QUADS, LANES * C], F32)
        hrelu = sb("hrelu", [P, LANES, C], F32)
        hT = sb("hT", [P, 2, 2, KC, P], F32)
        w_sb = sb("w_sb", [P, 2, KC, C], F32)
        ident = sb("ident", [P, P], F32)
        bias_sb = sb("bias_sb", [P, C], F32)
        differs = sb("differs", [P, HALF], U8)
        stats = sb("stats", [P, LANES, 6], F32)
        meanvar = sb("meanvar", [P, TILES, 2], F32)
        rowsum = sb("rowsum", [P, TILES, HALVES], F32)
        bad = sb("bad", [P, TILES * HALVES], F32)
        deg = sb("deg", [P, TILES], F32)
        mask = sb("mask", [P, TILES], F32)
        zin = sb("zin", [P, 2, LANES], F32)
        zrec = sb("zrec", [P, 2, LANES], F32)
        zroot = sb("zroot", [P, 2, LANES], F32)
        znew = sb("znew", [P, 2, LANES], F32)
        dinv_out = sb("dinv_out", [P, TILES], F32)
        c_in = sb("c_in", [P, TILES], F32)
        scale = sb("scale", [P, 6], F32)
        verdict = sb("verdict", [P, 4], F32)
        general_flag = sb("general_flag", [P, 1], I32)

        def first_word(t):
            q = t // LANES
            return sum(LANES * (QUADS - k) for k in range(q)) + (t % LANES) * (QUADS - q)

        def words(t, J0, J1):
            q = t // LANES
            if J1 <= q:
                return lower[:, (t // 2) % 2, t % 2, J0:J1, :]
            return upper[:, first_word(t) + J0 - q:first_word(t) + J1 - q, :]

        def weights8(t, J, b):
            w = words(t, J, J + 1).rearrange("p o m -> p (o m)")
            return w.bitcast(F8).rearrange("p (m b) -> p m b", b=LANES)[:, :, b]

        def part16(J, part):
            return gq[:, J, :].bitcast(F16)[:, part * LANES * C:(part + 1) * LANES * C]

        tr = ctx.enter_context(nc.psum_tensor("tr", [P, 2, 4, P], F32))
        ring = ctx.enter_context(nc.psum_tensor("ring", [P, RING, 2 * C], F32))

        w_in = sem("w_in")
        bias_in = sem("bias_in")
        x_in = [sem(f"x_in{q}") for q in range(QUADS)]
        adj_in = [sem(f"adj_in{k}") for k in range(STAGES)]
        xres_in = [sem(f"xres_in{q}") for q in range(QUADS)]
        ident_ready = sem("ident_ready")
        pool_step = sem("pool_step")
        wmax_ready = sem("wmax_ready")
        wmax_all = sem("wmax_all")
        scale_ready = sem("scale_ready")
        cast_done = sem("cast_done")
        check_done = sem("check_done")
        adj_turned = sem("adj_turned")
        words_ready = sem("words_ready")
        hrelu_ready = sem("hrelu_ready")
        h_turned = sem("h_turned")
        h_made = sem("h_made")
        act_evac = sem("act_evac")
        sums_made = sem("sums_made")
        sums_added = sem("sums_added")
        zrec_ready = sem("zrec_ready")
        root_ready = sem("root_ready")
        c_ready = sem("c_ready")
        acc_ready = sem("acc_ready")
        g_ready = sem("g_ready")
        verdict_ready = sem("verdict_ready")
        verdict_all = sem("verdict_all")
        flag_ready = sem("flag_ready")
        out_ready = sem("out_ready")
        out_done = sem("out_done")
        dve_step = sem("dve_step")
        gen_x_in = sem("gen_x_in")
        gen_relu_ready = sem("gen_relu_ready")
        gen_h_turned = sem("gen_h_turned")
        gen_hT_ready = sem("gen_hT_ready")
        gen_h_made = sem("gen_h_made")
        gen_g_ready = sem("gen_g_ready")
        gen_adj_in = sem("gen_adj_in")
        gen_turned = sem("gen_turned")
        gen_adjT_ready = sem("gen_adjT_ready")
        gen_sum_made = sem("gen_sum_made")
        gen_y_ready = sem("gen_y_ready")
        gen_stored = sem("gen_stored")
        gen_step = sem("gen_step")

        spare = upper[:].rearrange("p n m -> p (n m)").bitcast(F32)
        gen_g = spare[:, 0:TILES * C].rearrange("p (t c) -> p t c", c=C)
        gen_x, gen_relu, gen_y, gen_hT = [spare[:, (TILES + k) * C:(TILES + k + 1) * C] for k in range(4)]
        gen_adj = stage[:].rearrange("p s m -> p (s m)")[:, 0:N]
        gen_adjT = hT[:].rearrange("p e a k m -> p (e a k m)").rearrange("p (s m) -> p s m", s=2)
        gen_cin = zroot[:, 0, 0:1]

        def x_again(q):
            flat = stage[:].rearrange("p s m -> p (s m)")
            return flat[:, q * LANES * C:(q + 1) * LANES * C].rearrange("p (b c) -> p b c", b=LANES)

        finish_order = sorted(last_sum, key=lambda p: last_sum[p])

        def adj_is_general(eng):
            return eng.value_load(general_flag[0:1, 0:1], min_val=0, max_val=1) > 0

        def rows_of(dram, q, b):
            return dram[bass.ds(q, 1), :, b, :].rearrange("o w m -> (o w) m")

        block = ctx.enter_context(nc.Block())

        @block.sync
        def _(sp):
            sp.dma_start(acc[:, 0:LANES, :], x_q[0]).then_inc(x_in[0], 16)
            sp.dma_start(w_sb[:, 0], weightr.rearrange("(k p) c -> p k c", p=P)).then_inc(w_in, 16)
            sp.dma_start(w_sb[:, 1], weightd.rearrange("(k p) c -> p k c", p=P)).then_inc(w_in, 16)
            for n in range(TILES * HALVES):
                t, h = n // HALVES, n % HALVES
                if h == 0 and 1 <= t < QUADS:
                    sp.dma_start(acc[:, LANES * t:LANES * (t + 1), :], x_q[t]).then_inc(x_in[t], 16)
                if n >= STAGES:
                    sp.wait_ge(cast_done, n - STAGES + 1)
                    sp.wait_ge(check_done, n - STAGES + 1)
                sp.dma_start(stage[:, n % STAGES, :],
                             adj_q[t // LANES, :, t % LANES, h * HALF:(h + 1) * HALF]).then_inc(adj_in[n % STAGES], 16)
            sp.dma_start(bias_sb[:], bias.rearrange("(o c) -> o c", o=1).broadcast_to([P, C])).then_inc(bias_in, 16)
            sp.wait_ge(cast_done, TILES * HALVES)
            sp.wait_ge(check_done, TILES * HALVES)
            for q in range(QUADS):
                sp.dma_start(x_again(q), x_q[q]).then_inc(xres_in[q], 16)
            for n, p in enumerate(finish_order):
                sp.wait_ge(out_ready, n + 1)
                q, r = p // 2, p % 2
                sp.dma_start(out_q[q, :, 2 * r:2 * r + 2, :], acc[:, 2 * p:2 * p + 2, :]).then_inc(out_done, 16)
            sp.wait_ge(out_done, 16 * PAIRS)

        @block.gpsimd
        def _(pool):
            nc.gpsimd.memset(ident[:], 0.0).then_inc(pool_step, 1)
            pool.wait_ge(pool_step, 1)
            nc.gpsimd.affine_select(out=ident[:], in_=ident[:], compare_op=ALU.not_equal, fill=1.0, base=0,
                                    pattern=[[-1, P]], channel_multiplier=1).then_inc(ident_ready, 1)
            pool.wait_ge(wmax_ready, 1)
            nc.gpsimd.partition_all_reduce(scale[:, 1:2], scale[:, 0:1], P, RMAX).then_inc(wmax_all, 1)
            pool.wait_ge(verdict_ready, 1)
            nc.gpsimd.partition_all_reduce(verdict[:, 3:4], verdict[:, 2:3], P, RMAX).then_inc(verdict_all, 1)

        @block.scalar
        def _(act):
            ring_at = [0]

            def cast(t, h):
                n = HALVES * t + h
                act.wait_ge(adj_in[n % STAGES], 16 * (n // STAGES + 1))
                if t >= 2:
                    act.wait_ge(adj_turned, 2 * (t - 1))
                    act.wait_ge(check_done, HALVES * (t - 2) + h + 1)
                nc.scalar.activation(adj8[:, t % 2, h * HALF:(h + 1) * HALF], stage[:, n % STAGES, :], ACT.Copy,
                                     accum_out=rowsum[:, t, h:h + 1], saturate=False).then_inc(cast_done, 1)

            def take_words(t, bank):
                act.wait_ge(adj_turned, 2 * t + bank + 1)
                J0, J1, q = 4 * bank, 4 * bank + 4, t // LANES
                if bank == 0 and t % 2 == 0 and t // 2 - 2 >= 2:
                    act.wait_ge(sums_made, row_item[t // 2 - 2] + 1)
                cuts = sorted({J0, min(max(q, J0), J1), J1})
                ins = None
                for a, b in zip(cuts, cuts[1:]):
                    ins = nc.scalar.copy(words(t, a, b), tr[:, bank, a - J0:b - J0, :].bitcast(U32))
                ins.then_inc(words_ready, 1)

            def evacuate(item):
                kind, q, e = item
                n = ring_at[0]
                bank = ring[:, n % RING, :]
                if kind == "X":
                    act.wait_ge(h_turned, 2 * q + e + 1)
                    if q >= 1:
                        act.wait_ge(h_made, 2 * (q - 1) + e + 1)
                    nc.scalar.copy(hT[:, e].rearrange("p a k m -> p (a k m)"), bank).then_inc(act_evac, 1)
                else:
                    act.wait_ge(h_made, 2 * q + e + 1)
                    nc.scalar.copy(gq[:, q, e * 2 * C:(e + 1) * 2 * C], bank).then_inc(act_evac, 1)

            def slot(t, items):
                q = t // LANES - 1
                if t < TILES:
                    cast(t, 0)
                if t % LANES == 0 and q >= 0:
                    act.wait_ge(zrec_ready, q + 1)
                    nc.scalar.activation(zroot[:], zrec[:], ACT.Sqrt).then_inc(root_ready, 1)
                if 1 <= t <= TILES:
                    take_words(t - 1, 0)
                if t < TILES:
                    cast(t, 1)
                if 1 <= t <= TILES:
                    take_words(t - 1, 1)
                if t % LANES == 0 and q >= 0:
                    act.wait_ge(c_ready, q + 1)
                    act.wait_ge(act_evac, hw_count(q))
                    for b in range(LANES):
                        i = LANES * q + b
                        ins = nc.scalar.activation(acc[:, i, :], gq[:, q, b * C:(b + 1) * C], ACT.Copy,
                                                   scale=c_in[:, i:i + 1])
                    ins.then_inc(acc_ready, 1)
                for it in items:
                    if it[0] != "M":
                        evacuate(it)
                    ring_at[0] += 1

            def hw_count(q):
                return max(evac_count[n][1] for n, it in enumerate(ring_items) if it[0] == "H" and it[1] == q)

            for t in range(TILES + 1):
                slot(t, slots[t - 1] if t >= 1 else [])

            act.wait_ge(flag_ready, 1)
            with act.If(adj_is_general(act)):
                act.wait_ge(out_done, 16 * PAIRS)
                for w in range(2):
                    with act.Fori(w * QUADS // 2, (w + 1) * QUADS // 2) as q:
                        for b in range(LANES):
                            act.dma_start(gen_x, rows_of(x_q, q, b)).then_inc(gen_x_in, 16)
                            act.wait_ge(gen_relu_ready, q * LANES + (b + 1))
                with act.Fori(0, QUADS) as q:
                    for b in range(LANES):
                        act.dma_start(gen_adj, rows_of(adj_q, q, b)).then_inc(gen_adj_in, 16)
                        act.dma_start(gen_x, rows_of(x_q, q, b)).then_inc(gen_adj_in, 16)
                        act.wait_ge(gen_y_ready, q * LANES + (b + 1))
                        act.dma_start(rows_of(out_q, q, b), gen_y).then_inc(gen_stored, 16)
                        act.wait_ge(gen_stored, q * (16 * LANES) + 16 * (b + 1))

        @block.vector
        def _(dve):
            steps = [0]

            def step(ins):
                steps[0] += 1
                ins.then_inc(dve_step, 1)
                dve.wait_ge(dve_step, steps[0])

            def check(t, h):
                n = HALVES * t + h
                dve.wait_ge(cast_done, n + 1)
                if n:
                    dve.wait_ge(check_done, n)
                nc.vector.scalar_tensor_tensor(out=differs[:], in0=stage[:, n % STAGES, :], scalar=0.0,
                                               in1=adj8[:, t % 2, h * HALF:(h + 1) * HALF], op0=ALU.add,
                                               op1=ALU.not_equal, accum_out=bad[:, n:n + 1]).then_inc(check_done, 1)

            def norm(q):
                dve.wait_ge(x_in[q], 16)
                for b in range(LANES):
                    ins = nc.vector.bn_stats(stats[:, b, :], acc[:, LANES * q + b, :])
                step(ins)
                for b in range(LANES):
                    ins = nc.vector.bn_aggr(meanvar[:, LANES * q + b, :], stats[:, b, :])
                step(ins)
                if q >= 1:
                    dve.wait_ge(h_turned, 2 * q)
                for b in range(LANES):
                    i = LANES * q + b
                    ins = nc.vector.tensor_scalar(hrelu[:, b, :], acc[:, i, :], meanvar[:, i, 0:1], 0.0,
                                                  ALU.subtract, ALU.max)
                ins.then_inc(hrelu_ready, 1)

            def degrees(q):
                i0, i1 = LANES * q, LANES * (q + 1)
                dve.wait_ge(cast_done, HALVES * i1)
                step(nc.vector.scalar_tensor_tensor(out=deg[:, i0:i1], in0=rowsum[:, i0:i1, 0], scalar=1.0,
                                                    in1=rowsum[:, i0:i1, 1], op0=ALU.add, op1=ALU.add))
                nc.vector.tensor_scalar(mask[:, i0:i1], deg[:, i0:i1], 0.0, None, ALU.is_gt)
                step(nc.vector.tensor_scalar(zin[:, 0, :], deg[:, i0:i1], DEG_FLOOR, None, ALU.max))
                step(nc.vector.scalar_tensor_tensor(out=zin[:, 1, :], in0=meanvar[:, i0:i1, 1], scalar=EPS,
                                                    in1=zin[:, 0, :], op0=ALU.add, op1=ALU.mult))
                nc.vector.reciprocal(zrec[:], zin[:]).then_inc(zrec_ready, 1)

            def roots(q):
                i0, i1 = LANES * q, LANES * (q + 1)
                dve.wait_ge(root_ready, q + 1)
                step(nc.vector.tensor_tensor(znew[:], zroot[:], zroot[:], ALU.mult))
                step(nc.vector.tensor_tensor(znew[:], znew[:], zin[:], ALU.mult))
                step(nc.vector.tensor_scalar(znew[:], znew[:], -0.5, 1.5, ALU.mult, ALU.add))
                step(nc.vector.tensor_tensor(znew[:], znew[:], zroot[:], ALU.mult))
                nc.vector.scalar_tensor_tensor(out=dinv_out[:, i0:i1], in0=znew[:, 0, :], scalar=scale[:, 4:5],
                                               in1=mask[:, i0:i1], op0=ALU.mult, op1=ALU.mult)
                nc.vector.scalar_tensor_tensor(out=c_in[:, i0:i1], in0=znew[:, 1, :], scalar=scale[:, 3:4],
                                               in1=mask[:, i0:i1], op0=ALU.mult, op1=ALU.mult).then_inc(c_ready, 1)

            def split(q):
                dve.wait_ge(acc_ready, q + 1)
                whole = acc[:, LANES * q:LANES * (q + 1), :].rearrange("p b c -> p (b c)")
                step(nc.vector.tensor_copy(part16(q, 0), whole))
                nc.vector.tensor_tensor(part16(q, 1), whole, part16(q, 0), ALU.subtract).then_inc(g_ready, 1)

            sums_at = [0]

            def add_sums():
                k = sums_at[0]
                sums_at[0] += 1
                n = sums[k]
                p = ring_items[n][1]
                pair = acc[:, 2 * p:2 * p + 2, :].rearrange("p b c -> p (b c)")
                dve.wait_ge(sums_made, k + 1)
                dve.wait_ge(g_ready, p // 2 + 1)
                if k:
                    dve.wait_ge(sums_added, k)
                nc.vector.tensor_tensor(pair, pair, ring[:, bank_of[n], :], ALU.add).then_inc(sums_added, 1)
                if last_sum[p] == k:
                    finish(p, k)

            def finish(p, k):
                pair = acc[:, 2 * p:2 * p + 2, :].rearrange("p b c -> p (b c)")
                if p == finish_order[0]:
                    dve.wait_ge(bias_in, 16)
                dve.wait_ge(sums_added, k + 1)
                for i in (2 * p, 2 * p + 1):
                    ins = nc.vector.scalar_tensor_tensor(out=acc[:, i, :], in0=acc[:, i, :],
                                                         scalar=dinv_out[:, i:i + 1], in1=bias_sb[:],
                                                         op0=ALU.mult, op1=ALU.add)
                step(ins)
                step(nc.vector.scalar_tensor_tensor(out=pair, in0=pair, scalar=SLOPE, in1=pair,
                                                    op0=ALU.mult, op1=ALU.max))
                dve.wait_ge(xres_in[p // 2], 16)
                again = x_again(p // 2)[:, 2 * (p % 2):2 * (p % 2) + 2, :].rearrange("p b c -> p (b c)")
                nc.vector.tensor_tensor(pair, pair, again, ALU.add).then_inc(out_ready, 1)

            dve.wait_ge(w_in, 32)
            nc.vector.tensor_reduce(scale[:, 0:1], w_sb[:].rearrange("p a k c -> p (a k c)"), AX_X, ALU.max,
                                    apply_absolute_value=True).then_inc(wmax_ready, 1)
            norm(0)
            dve.wait_ge(wmax_all, 1)
            step(nc.vector.tensor_scalar(scale[:, 2:3].bitcast(U32), scale[:, 1:2].bitcast(U32), EXP_MASK, None,
                                         ALU.bitwise_and))
            step(nc.vector.tensor_scalar(scale[:, 2:3], scale[:, 2:3], 2.0 ** -60, 2.0 ** 60, ALU.max, ALU.min))
            step(nc.vector.reciprocal(scale[:, 3:4], scale[:, 2:3]))
            step(nc.vector.tensor_scalar(scale[:, 3:4], scale[:, 3:4], 64.0, None, ALU.mult))
            step(nc.vector.tensor_scalar(scale[:, 4:5], scale[:, 2:3], 1.0 / 64.0, None, ALU.mult))

            due, at = {}, 0
            for t, items in enumerate(slots):
                for it in items:
                    if it[0] == "M":
                        at = max(at, t + 1, LANES * (it[1] // 2) + LANES + 1)
                        due.setdefault(at, []).append(it)
            for t in range(TILES + 2):
                q = t // LANES - 1
                if t % LANES == 0 and q >= 0:
                    degrees(q)
                if t % LANES == 1 and q >= 0:
                    split(q)
                if t < TILES:
                    check(t, 0)
                mine = due.get(t, [])
                for _ in mine[:len(mine) // 2]:
                    add_sums()
                if t % LANES == 0 and q >= 0:
                    roots(q)
                if 1 <= t < QUADS:
                    norm(t)
                if t < TILES:
                    check(t, 1)
                for _ in mine[len(mine) // 2:]:
                    add_sums()
                if t == TILES:
                    dve.wait_ge(check_done, TILES * HALVES)
                    nc.vector.tensor_reduce(verdict[:, 0:1], bad[:], AX_X, ALU.max)
                    step(nc.vector.tensor_reduce(verdict[:, 1:2], deg[:], AX_X, ALU.min))
                    step(nc.vector.tensor_scalar(verdict[:, 1:2], verdict[:, 1:2], 1.0, None, ALU.is_lt))
                    nc.vector.tensor_tensor(verdict[:, 2:3], verdict[:, 0:1], verdict[:, 1:2],
                                            ALU.max).then_inc(verdict_ready, 1)
            while sums_at[0] < len(sums):
                add_sums()
                if sums_at[0] == len(sums) - 2:
                    dve.wait_ge(verdict_all, 1)
                    nc.vector.tensor_scalar(general_flag[:], verdict[:, 3:4], 0.0, None, ALU.is_gt).then_inc(flag_ready, 1)

            dve.wait_ge(flag_ready, 1)
            with dve.If(adj_is_general(dve)):
                nc.vector.tensor_scalar(c_in[:], c_in[:], scale[:, 4:5], None, ALU.mult).then_inc(gen_step, 1)
                nc.vector.tensor_scalar(dinv_out[:], dinv_out[:], scale[:, 3:4], None, ALU.mult).then_inc(gen_step, 1)
                dve.wait_ge(gen_step, 2)
                for w in range(2):
                    with dve.Fori(w * QUADS // 2, (w + 1) * QUADS // 2) as q:
                        for b in range(LANES):
                            i = q * LANES + b
                            dve.wait_ge(gen_x_in, q * (16 * LANES) + 16 * (b + 1))
                            nc.vector.tensor_scalar(gen_relu, gen_x, meanvar[:, bass.ds(i, 1), 0], 0.0,
                                                    ALU.subtract, ALU.max).then_inc(gen_relu_ready, 1)
                            dve.wait_ge(gen_h_turned, i + 1)
                            nc.vector.tensor_copy(gen_hT, ring[:, 0, 0:C]).then_inc(gen_hT_ready, 1)
                            dve.wait_ge(gen_h_made, i + 1)
                            nc.vector.tensor_scalar(gen_g[:, bass.ds(i, 1), :].rearrange("p o c -> p (o c)"),
                                                    ring[:, 1, 0:C], c_in[:, bass.ds(i, 1)], None,
                                                    ALU.mult).then_inc(gen_g_ready, 1)
                with dve.Fori(0, QUADS) as q:
                    for b in range(LANES):
                        i = q * LANES + b
                        for k in range(TILES // 4):
                            dve.wait_ge(gen_turned, i * (TILES // 4) + (k + 1))
                            nc.vector.tensor_copy(gen_adjT[:, k % 2, :], ring[:, k % 2, :]).then_inc(gen_adjT_ready, 1)
                        dve.wait_ge(gen_sum_made, i + 1)
                        dve.wait_ge(gen_adj_in, q * (32 * LANES) + 32 * (b + 1))
                        nc.vector.tensor_tensor(gen_y, gen_g[:, bass.ds(i, 1), :].rearrange("p o c -> p (o c)"),
                                                ring[:, 2, 0:C], ALU.add).then_inc(gen_step, 1)
                        dve.wait_ge(gen_step, i * 3 + 3)
                        nc.vector.scalar_tensor_tensor(out=gen_y, in0=gen_y, scalar=dinv_out[:, bass.ds(i, 1)],
                                                       in1=bias_sb[:], op0=ALU.mult, op1=ALU.add).then_inc(gen_step, 1)
                        dve.wait_ge(gen_step, i * 3 + 4)
                        nc.vector.scalar_tensor_tensor(out=gen_y, in0=gen_y, scalar=SLOPE, in1=gen_y,
                                                       op0=ALU.mult, op1=ALU.max).then_inc(gen_step, 1)
                        dve.wait_ge(gen_step, i * 3 + 5)
                        nc.vector.tensor_tensor(gen_y, gen_y, gen_x, ALU.add).then_inc(gen_y_ready, 1)

        @block.tensor
        def _(pe):
            ring_at = [0]

            def turn_adj(t):
                for bank in range(2):
                    if bank == 0:
                        pe.wait_ge(cast_done, HALVES * t + 1)
                    else:
                        pe.wait_ge(cast_done, HALVES * t + 2)
                    if t:
                        pe.wait_ge(words_ready, 2 * (t - 1) + bank + 1)
                    for k in range(4):
                        J = 4 * bank + k
                        ins = pe.transpose(tr[:, bank, k, :],
                                           adj8[:, t % 2, J * LANES * P:(J + 1) * LANES * P].bitcast(F32), ident[:])
                    ins.then_inc(adj_turned, 1)

            def item(it):
                n = ring_at[0]
                ring_at[0] += 1
                bank = ring[:, bank_of[n], :]
                if n >= RING:
                    who, count = evac_count[n - RING]
                    pe.wait_ge(act_evac if who == "act" else sums_added, count)
                if it[0] == "X":
                    _, q, e = it
                    pe.wait_ge(hrelu_ready, q + 1)
                    for a in range(2):
                        for k in range(KC):
                            at = (a * KC + k) * P
                            ins = pe.transpose(bank[:, at:at + P], hrelu[:, 2 * e + a, k * P:(k + 1) * P], ident[:])
                    ins.then_inc(h_turned, 1)
                elif it[0] == "H":
                    _, q, e = it
                    pe.wait_ge(act_evac, evac_count[ring_items.index(("X", q, e))][1])
                    w = 0 if q < QUADS // 2 else 1
                    for a in range(2):
                        for k in range(KC):
                            ins = pe.matmul(bank[:, a * C:(a + 1) * C], hT[:, e, a, k, :], w_sb[:, w, k, :],
                                            start=(k == 0), stop=(k == KC - 1))
                    ins.then_inc(h_made, 1)
                else:
                    _, p, Js = it
                    pe.wait_ge(words_ready, 2 * (2 * p + 1) + 2)
                    pe.wait_ge(g_ready, Js[-1] + 1)
                    for a in range(2):
                        for J in Js:
                            for b in range(LANES):
                                for part in range(2):
                                    ins = pe.matmul(bank[:, a * C:(a + 1) * C], weights8(2 * p + a, J, b),
                                                    part16(J, part)[:, b * C:(b + 1) * C],
                                                    start=(J == Js[0] and b == 0 and part == 0),
                                                    stop=(J == Js[-1] and b == LANES - 1 and part == 1))
                    ins.then_inc(sums_made, 1)

            pe.wait_ge(ident_ready, 1)
            pe.wait_ge(w_in, 32)
            for t, items in enumerate(slots):
                if t < TILES:
                    turn_adj(t)
                for it in items:
                    item(it)
            for it in rest:
                item(it)

            pe.wait_ge(flag_ready, 1)
            with pe.If(adj_is_general(pe)):
                pe.wait_ge(sums_added, len(sums))
                for w in range(2):
                    with pe.Fori(w * QUADS // 2, (w + 1) * QUADS // 2) as q:
                        for b in range(LANES):
                            i = q * LANES + b
                            pe.wait_ge(gen_relu_ready, i + 1)
                            for k in range(KC):
                                ins = pe.transpose(ring[:, 0, k * P:(k + 1) * P], gen_relu[:, k * P:(k + 1) * P],
                                                   ident[:])
                            ins.then_inc(gen_h_turned, 1)
                            pe.wait_ge(gen_hT_ready, i + 1)
                            for k in range(KC):
                                ins = pe.matmul(ring[:, 1, 0:C], gen_hT[:, k * P:(k + 1) * P], w_sb[:, w, k, :],
                                                start=(k == 0), stop=(k == KC - 1))
                            ins.then_inc(gen_h_made, 1)
                pe.wait_ge(gen_g_ready, TILES)
                with pe.Fori(0, QUADS) as q:
                    for b in range(LANES):
                        i = q * LANES + b
                        pe.wait_ge(gen_adj_in, q * (32 * LANES) + 32 * (b + 1))
                        for k in range(TILES // 4 + 1):
                            if k < TILES // 4:
                                if k >= 2:
                                    pe.wait_ge(gen_adjT_ready, i * (TILES // 4) + (k - 1))
                                cols = gen_adj[:, k * 4 * P:(k + 1) * 4 * P].rearrange("p (w j) -> p j w", j=4)
                                for j in range(4):
                                    ins = pe.transpose(ring[:, k % 2, j * P:(j + 1) * P], cols[:, j, :], ident[:])
                                ins.then_inc(gen_turned, 1)
                            if k >= 1:
                                pe.wait_ge(gen_adjT_ready, i * (TILES // 4) + k)
                                for j in range(4):
                                    ins = pe.matmul(ring[:, 2, 0:C], gen_adjT[:, (k - 1) % 2, j * P:(j + 1) * P],
                                                    gen_g[:, 4 * (k - 1) + j, :], start=(k == 1 and j == 0),
                                                    stop=(k == TILES // 4 and j == 3))
                        ins.then_inc(gen_sum_made, 1)


_INS = ["x", "adj", "L0_gnn_weightr", "L0_gnn_weightd", "L0_gnn_bias"]
_OUT = ((4096, 256), "float32")


def kernel(**inputs):
    import numpy as _np
    import concourse.bacc as _bacc
    from concourse import mybir as _mybir
    from concourse.bass_utils import run_bass_kernel_spmd as _run

    nc = _bacc.Bacc("TRN2", target_bir_lowering=False, num_devices=1)
    arrays, args = {}, []
    for name in _INS:
        a = _np.ascontiguousarray(inputs[name])
        arrays[f"in_{name}_dram"] = a
        args.append(nc.dram_tensor(f"in_{name}_dram", a.shape, _mybir.dt.from_np(a.dtype), kind="ExternalInput").ap())
    dt = _mybir.dt.from_np(_np.dtype(_OUT[1]))
    args.append(nc.dram_tensor("out_0_dram", _OUT[0], dt, kind="ExternalOutput").ap())
    gnn_layer(nc, *args)
    r = _run(nc, [arrays], core_ids=[0])
    return r.results[0]["out_0_dram"]
```

```python
from contextlib import ExitStack

import concourse.bass as bass
from concourse import mybir

F32 = mybir.dt.float32
F16 = mybir.dt.float16
F8 = mybir.dt.float8e4
U32 = mybir.dt.uint32
I32 = mybir.dt.int32
U8 = mybir.dt.uint8
ALU = mybir.AluOpType
ACT = mybir.ActivationFunctionType
AX_X = mybir.AxisListType.X
RMAX = bass.bass_isa.ReduceOp.max

P = 128
LANES = 4
EPS = 1e-5
SLOPE = 0.01
DEG_FLOOR = 2.0 ** -100
EXP_MASK = 0x7F800000
RING = 6
HALVES = 2
H_RATE = 1
FILL, OVER = 0.8, 1.8
REST_FIRST = 4
G_FIRST = 3
G_LAG = 1
LOAD_US, BLOCK_US = 6.6, 0.216
EARLY, LEAST = 12, 2
STAGES = 4


def h_slot(q):
    return 1 + q // H_RATE


def g_slot(u):
    return max(2 * u + 2, G_FIRST)


def plan_products(tiles):
    quads, pairs = tiles // LANES, tiles // 2
    own = {p: LANES // 2 * (p // (LANES // 2)) for p in range(pairs)}
    todo = {p: list(range(own[p], pairs)) for p in range(pairs)}
    slots, clock = [], 0.0
    for t in range(tiles + 2):
        items = []
        clock = max(clock, LOAD_US * t) + 0.9
        for q in range(quads):
            if t == h_slot(q):
                items += [("X", q, 0), ("X", q, 1)] + [("H", q - 1, 0), ("H", q - 1, 1)] * (q > 0)
                clock += 4.5
        if t == h_slot(quads - 1) + 1:
            items += [("H", quads - 1, 0), ("H", quads - 1, 1)]
            clock += 3.5
        p = (t - 3) // 2
        if t % 2 == 1 and p >= 0 and own[p]:
            items.append(("M", p, list(range(own[p]))))
            clock += 4 * own[p] * BLOCK_US
        while t < tiles:
            ready = [(len([u for u in us if g_slot(u) + G_LAG <= t]), -p) for p, us in todo.items() if 2 * p + 3 <= t]
            n, p = max(ready, default=(0, 0))
            late = clock > LOAD_US * (t + FILL) and (items or clock > LOAD_US * (t + OVER))
            if n < (1 if t < EARLY else LEAST) or late:
                break
            us, todo[-p] = todo[-p][:n], todo[-p][n:]
            items.append(("M", -p, us))
            clock += 4 * n * BLOCK_US
        slots.append(items)
    rest = sorted((p for p in todo if todo[p]), key=lambda p: -len(todo[p]))
    rest = rest[:REST_FIRST] + rest[:REST_FIRST - 1:-1]
    return slots, [("M", p, todo[p]) for p in rest]


def gnn_layer(nc, x, adj, weightr, weightd, bias, out):
    N, C = x.shape
    TILES = N // P
    QUADS = TILES // LANES
    PAIRS = TILES // 2
    WORDS = N // LANES // P
    KC = C // P
    HALF = N // HALVES
    assert C == 2 * P and WORDS == QUADS and N % (LANES * P) == 0

    x_q = x.rearrange("(q w b) c -> q w b c", w=P, b=LANES)
    out_q = out.rearrange("(q w b) c -> q w b c", w=P, b=LANES)
    adj_q = adj.rearrange("(q w b) m -> q w b m", w=P, b=LANES)

    slots, rest = plan_products(TILES)
    ring_items = [it for s in slots for it in s] + rest
    bank_of, evac_count, seen = [], [], {"act": 0, "dve": 0}
    for n, it in enumerate(ring_items):
        who = "dve" if it[0] == "M" else "act"
        seen[who] += 1
        bank_of.append(n % RING)
        evac_count.append((who, seen[who]))
    sums = [n for n, it in enumerate(ring_items) if it[0] == "M"]
    last_sum = {ring_items[n][1]: k for k, n in enumerate(sums)}
    row_item = {}
    for k, n in enumerate(sums):
        row_item.setdefault(ring_items[n][1], k)

    with ExitStack() as ctx:
        def sb(name, shape, dt):
            return ctx.enter_context(nc.sbuf_tensor(name, shape, dt))

        def sem(name):
            return ctx.enter_context(nc.semaphore(name))

        stage = sb("stage", [P, STAGES, HALF], F32)
        adj8 = sb("adj8", [P, 2, N], F8)
        upper_words = sum(LANES * (QUADS - q) for q in range(QUADS))
        upper = sb("upper", [P, upper_words, P], U32)
        lower = sb("lower", [P, 2, 2, QUADS - 1, P], U32)
        acc = sb("acc", [P, TILES, C], F32)
        gq = sb("gq", [P, QUADS, LANES * C], F32)
        centre = sb("centre", [P, LANES, C], F32)
        hT = sb("hT", [P, 2, 2, KC, P], F32)
        w_sb = sb("w_sb", [P, 2, KC, C], F32)
        ident = sb("ident", [P, P], F32)
        bias_sb = sb("bias_sb", [P, C], F32)
        differs = sb("differs", [P, HALF], U8)
        stats = sb("stats", [P, LANES, 6], F32)
        meanvar = sb("meanvar", [P, TILES, 2], F32)
        rowsum = sb("rowsum", [P, TILES, HALVES], F32)
        bad = sb("bad", [P, TILES * HALVES], F32)
        deg = sb("deg", [P, TILES], F32)
        mask = sb("mask", [P, TILES], F32)
        zin = sb("zin", [P, 2, 2], F32)
        zrec = sb("zrec", [P, 2, 2], F32)
        zroot = sb("zroot", [P, 2, 2], F32)
        znew = sb("znew", [P, 2, 2], F32)
        dinv_out = sb("dinv_out", [P, TILES], F32)
        c_in = sb("c_in", [P, TILES], F32)
        scale = sb("scale", [P, 6], F32)
        verdict = sb("verdict", [P, 4], F32)
        general_flag = sb("general_flag", [P, 1], I32)

        def first_word(t):
            q = t // LANES
            return sum(LANES * (QUADS - k) for k in range(q)) + (t % LANES) * (QUADS - q)

        def words(t, J0, J1):
            q = t // LANES
            if J1 <= q:
                return lower[:, (t // 2) % 2, t % 2, J0:J1, :]
            return upper[:, first_word(t) + J0 - q:first_word(t) + J1 - q, :]

        def weights8(t, J, b):
            w = words(t, J, J + 1).rearrange("p o m -> p (o m)")
            return w.bitcast(F8).rearrange("p (m b) -> p m b", b=LANES)[:, :, b]

        def part16(u, part):
            at = (u % 2) * 2 * C
            return gq[:, u // 2, at:at + 2 * C].bitcast(F16)[:, part * 2 * C:(part + 1) * 2 * C]

        tr = ctx.enter_context(nc.psum_tensor("tr", [P, 2, 4, P], F32))
        ring = ctx.enter_context(nc.psum_tensor("ring", [P, RING, 2 * C], F32))

        w_in = sem("w_in")
        bias_in = sem("bias_in")
        x_in = [sem(f"x_in{q}") for q in range(QUADS)]
        adj_in = [sem(f"adj_in{k}") for k in range(STAGES)]
        xres_in = [sem(f"xres_in{q}") for q in range(QUADS)]
        ident_ready = sem("ident_ready")
        pool_step = sem("pool_step")
        wmax_ready = sem("wmax_ready")
        wmax_all = sem("wmax_all")
        scale_ready = sem("scale_ready")
        cast_done = sem("cast_done")
        check_done = sem("check_done")
        adj_turned = sem("adj_turned")
        words_ready = sem("words_ready")
        mean_ready = sem("mean_ready")
        centred = sem("centred")
        h_turned = sem("h_turned")
        h_made = sem("h_made")
        act_evac = sem("act_evac")
        sums_made = sem("sums_made")
        sums_added = sem("sums_added")
        zrec_ready = sem("zrec_ready")
        root_warm = sem("root_warm")
        root_ready = sem("root_ready")
        acc_ready = sem("acc_ready")
        high_ready = sem("high_ready")
        g_ready = sem("g_ready")
        verdict_ready = sem("verdict_ready")
        verdict_all = sem("verdict_all")
        flag_ready = sem("flag_ready")
        out_ready = sem("out_ready")
        out_done = sem("out_done")
        dve_step = sem("dve_step")
        gen_x_in = sem("gen_x_in")
        gen_relu_ready = sem("gen_relu_ready")
        gen_h_turned = sem("gen_h_turned")
        gen_hT_ready = sem("gen_hT_ready")
        gen_h_made = sem("gen_h_made")
        gen_g_ready = sem("gen_g_ready")
        gen_adj_in = sem("gen_adj_in")
        gen_turned = sem("gen_turned")
        gen_adjT_ready = sem("gen_adjT_ready")
        gen_sum_made = sem("gen_sum_made")
        gen_y_ready = sem("gen_y_ready")
        gen_stored = sem("gen_stored")
        gen_step = sem("gen_step")

        spare = upper[:].rearrange("p n m -> p (n m)").bitcast(F32)
        gen_g = spare[:, 0:TILES * C].rearrange("p (t c) -> p t c", c=C)
        gen_x, gen_relu, gen_y, gen_hT = [spare[:, (TILES + k) * C:(TILES + k + 1) * C] for k in range(4)]
        gen_adj = stage[:].rearrange("p s m -> p (s m)")[:, 0:N]
        gen_adjT = hT[:].rearrange("p e a k m -> p (e a k m)").rearrange("p (s m) -> p s m", s=2)

        def x_again(q):
            flat = stage[:].rearrange("p s m -> p (s m)")
            return flat[:, q * LANES * C:(q + 1) * LANES * C].rearrange("p (b c) -> p b c", b=LANES)

        finish_order = sorted(last_sum, key=lambda p: last_sum[p])

        def hw_count(q):
            return max(evac_count[n][1] for n, it in enumerate(ring_items) if it[0] == "H" and it[1] == q)

        def pair(p):
            return acc[:, 2 * p:2 * p + 2, :].rearrange("p b c -> p (b c)")

        def adj_is_general(eng):
            return eng.value_load(general_flag[0:1, 0:1], min_val=0, max_val=1) > 0

        def rows_of(dram, q, b):
            return dram[bass.ds(q, 1), :, b, :].rearrange("o w m -> (o w) m")

        block = ctx.enter_context(nc.Block())

        @block.sync
        def _(sp):
            for n in range(TILES * HALVES):
                t, h = n // HALVES, n % HALVES
                if n >= STAGES:
                    sp.wait_ge(cast_done, n - STAGES + 1)
                    sp.wait_ge(check_done, n - STAGES + 1)
                sp.dma_start(stage[:, n % STAGES, :],
                             adj_q[t // LANES, :, t % LANES, h * HALF:(h + 1) * HALF]).then_inc(adj_in[n % STAGES], 16)
                for q in range(QUADS):
                    if n == max(0, HALVES * (h_slot(q) - 2) + 1):
                        sp.dma_start(acc[:, LANES * q:LANES * (q + 1), :], x_q[q]).then_inc(x_in[q], 16)
                if n == 1:
                    sp.dma_start(w_sb[:, 0], weightr.rearrange("(k p) c -> p k c", p=P)).then_inc(w_in, 16)
                    sp.dma_start(w_sb[:, 1], weightd.rearrange("(k p) c -> p k c", p=P)).then_inc(w_in, 16)
            sp.dma_start(bias_sb[:], bias.rearrange("(o c) -> o c", o=1).broadcast_to([P, C])).then_inc(bias_in, 16)
            sp.wait_ge(cast_done, TILES * HALVES)
            sp.wait_ge(check_done, TILES * HALVES)
            for q in range(QUADS):
                sp.dma_start(x_again(q), x_q[q]).then_inc(xres_in[q], 16)
            for n, p in enumerate(finish_order):
                sp.wait_ge(out_ready, n + 1)
                q, r = p // 2, p % 2
                sp.dma_start(out_q[q, :, 2 * r:2 * r + 2, :], acc[:, 2 * p:2 * p + 2, :]).then_inc(out_done, 16)
            sp.wait_ge(out_done, 16 * PAIRS)

        @block.gpsimd
        def _(pool):
            nc.gpsimd.memset(ident[:], 0.0).then_inc(pool_step, 1)
            pool.wait_ge(pool_step, 1)
            nc.gpsimd.affine_select(out=ident[:], in_=ident[:], compare_op=ALU.not_equal, fill=1.0, base=0,
                                    pattern=[[-1, P]], channel_multiplier=1).then_inc(ident_ready, 1)
            pool_steps = [1]

            def step(ins):
                pool_steps[0] += 1
                ins.then_inc(pool_step, 1)
                pool.wait_ge(pool_step, pool_steps[0])

            def centre_rows(q):
                pool.wait_ge(mean_ready, q + 1)
                if q:
                    pool.wait_ge(h_turned, 2 * q)
                for b in range(LANES):
                    i = LANES * q + b
                    ins = nc.gpsimd.tensor_scalar(centre[:, b, :], acc[:, i, :], -1.0, meanvar[:, i, 0:1],
                                                  ALU.mult, ALU.add)
                ins.then_inc(centred, 1)

            def roots(u):
                i0, i1 = 2 * u, 2 * u + 2
                pool.wait_ge(root_ready, u + 1)
                if u == 0:
                    pool.wait_ge(scale_ready, 1)
                step(nc.gpsimd.tensor_tensor(znew[:], zroot[:], zroot[:], ALU.mult))
                step(nc.gpsimd.tensor_tensor(znew[:], znew[:], zin[:], ALU.mult))
                step(nc.gpsimd.tensor_scalar(znew[:], znew[:], -0.5, 1.5, ALU.mult, ALU.add))
                step(nc.gpsimd.tensor_tensor(znew[:], znew[:], zroot[:], ALU.mult))
                nc.gpsimd.tensor_tensor(dinv_out[:, i0:i1], znew[:, 0, :], mask[:, i0:i1], ALU.mult)
                step(nc.gpsimd.tensor_tensor(c_in[:, i0:i1], znew[:, 1, :], mask[:, i0:i1], ALU.mult))
                nc.gpsimd.tensor_scalar(dinv_out[:, i0:i1], dinv_out[:, i0:i1], scale[:, 4:5], 0.0, ALU.mult, ALU.add)
                step(nc.gpsimd.tensor_scalar(c_in[:, i0:i1], c_in[:, i0:i1], scale[:, 3:4], 0.0, ALU.mult, ALU.add))

            def scaled_rows(u):
                if u % 2 == 0:
                    pool.wait_ge(act_evac, hw_count(u // 2))
                    pool.wait_ge(centred, u // 2 + 1)
                for i in (2 * u, 2 * u + 1):
                    b = i % LANES
                    ins = nc.gpsimd.tensor_scalar(acc[:, i, :], gq[:, u // 2, b * C:(b + 1) * C], c_in[:, i:i + 1],
                                                  0.0, ALU.mult, ALU.add)
                ins.then_inc(acc_ready, 1)

            def low_part(u):
                pool.wait_ge(high_ready, u + 1)
                pool.wait_ge(acc_ready, u + 1)
                nc.gpsimd.tensor_tensor(part16(u, 1), pair(u), part16(u, 0), ALU.subtract).then_inc(g_ready, 1)

            for t in range(TILES + 1):
                if t == 0:
                    centre_rows(0)
                    pool.wait_ge(wmax_ready, 1)
                    nc.gpsimd.partition_all_reduce(scale[:, 1:2], scale[:, 0:1], P, RMAX).then_inc(wmax_all, 1)
                mine = [u for u in range(PAIRS) if g_slot(u) == t]
                for u in mine:
                    roots(u)
                    scaled_rows(u)
                    if u == mine[-1]:
                        for k in range(1, QUADS):
                            if t == h_slot(k) - 1:
                                centre_rows(k)
                    low_part(u)
                if not mine:
                    for k in range(1, QUADS):
                        if t == h_slot(k) - 1:
                            centre_rows(k)
            pool.wait_ge(verdict_ready, 1)
            nc.gpsimd.partition_all_reduce(verdict[:, 3:4], verdict[:, 2:3], P, RMAX).then_inc(verdict_all, 1)

        @block.scalar
        def _(act):
            ring_at = [0]

            def cast(t, h):
                n = HALVES * t + h
                act.wait_ge(adj_in[n % STAGES], 16 * (n // STAGES + 1))
                if t >= 2:
                    act.wait_ge(adj_turned, 2 * (t - 1))
                    act.wait_ge(check_done, HALVES * (t - 2) + h + 1)
                nc.scalar.activation(adj8[:, t % 2, h * HALF:(h + 1) * HALF], stage[:, n % STAGES, :], ACT.Copy,
                                     accum_out=rowsum[:, t, h:h + 1], saturate=False).then_inc(cast_done, 1)

            def take_words(t, bank):
                act.wait_ge(adj_turned, 2 * t + bank + 1)
                J0, J1, q = 4 * bank, 4 * bank + 4, t // LANES
                if bank == 0 and t % 2 == 0 and t // 2 - 2 >= 2:
                    act.wait_ge(sums_made, row_item[t // 2 - 2] + 1)
                cuts = sorted({J0, min(max(q, J0), J1), J1})
                ins = None
                for a, b in zip(cuts, cuts[1:]):
                    ins = nc.scalar.copy(words(t, a, b), tr[:, bank, a - J0:b - J0, :].bitcast(U32))
                ins.then_inc(words_ready, 1)

            def evacuate(item):
                kind, q, e = item
                n = ring_at[0]
                bank = ring[:, n % RING, :]
                if kind == "X":
                    act.wait_ge(h_turned, 2 * q + e + 1)
                    if q >= 1:
                        act.wait_ge(h_made, 2 * (q - 1) + e + 1)
                    nc.scalar.activation(hT[:, e].rearrange("p a k m -> p (a k m)"), bank, ACT.Relu,
                                         scale=-1.0).then_inc(act_evac, 1)
                else:
                    act.wait_ge(h_made, 2 * q + e + 1)
                    nc.scalar.copy(gq[:, q, e * 2 * C:(e + 1) * 2 * C], bank).then_inc(act_evac, 1)

            def slot(t, items):
                if t < TILES:
                    cast(t, 0)
                if 1 <= t <= TILES:
                    take_words(t - 1, 0)
                if t < TILES:
                    cast(t, 1)
                for u in range(PAIRS):
                    if t == g_slot(u):
                        act.wait_ge(zrec_ready, u + 1)
                        if u:
                            act.wait_ge(acc_ready, u)
                        nc.scalar.activation(zroot[:], zrec[:], ACT.Sqrt).then_inc(root_ready, 1)
                if 1 <= t <= TILES:
                    take_words(t - 1, 1)
                for it in items:
                    if it[0] != "M":
                        evacuate(it)
                    ring_at[0] += 1

            act.wait_ge(ident_ready, 1)
            nc.scalar.activation(zroot[:, 0, 0:1], ident[:, 0:1], ACT.Sqrt).then_inc(root_warm, 1)
            act.wait_ge(root_warm, 1)
            for t in range(TILES + 1):
                slot(t, slots[t - 1] if t >= 1 else [])

            act.wait_ge(flag_ready, 1)
            with act.If(adj_is_general(act)):
                act.wait_ge(out_done, 16 * PAIRS)
                for w in range(2):
                    with act.Fori(w * QUADS // 2, (w + 1) * QUADS // 2) as q:
                        for b in range(LANES):
                            act.dma_start(gen_x, rows_of(x_q, q, b)).then_inc(gen_x_in, 16)
                            act.wait_ge(gen_relu_ready, q * LANES + (b + 1))
                with act.Fori(0, QUADS) as q:
                    for b in range(LANES):
                        act.dma_start(gen_adj, rows_of(adj_q, q, b)).then_inc(gen_adj_in, 16)
                        act.dma_start(gen_x, rows_of(x_q, q, b)).then_inc(gen_adj_in, 16)
                        act.wait_ge(gen_y_ready, q * LANES + (b + 1))
                        act.dma_start(rows_of(out_q, q, b), gen_y).then_inc(gen_stored, 16)
                        act.wait_ge(gen_stored, q * (16 * LANES) + 16 * (b + 1))

        @block.vector
        def _(dve):
            steps = [0]

            def step(ins):
                steps[0] += 1
                ins.then_inc(dve_step, 1)
                dve.wait_ge(dve_step, steps[0])

            def check(t, h):
                n = HALVES * t + h
                dve.wait_ge(cast_done, n + 1)
                if n:
                    dve.wait_ge(check_done, n)
                nc.vector.scalar_tensor_tensor(out=differs[:], in0=stage[:, n % STAGES, :], scalar=0.0,
                                               in1=adj8[:, t % 2, h * HALF:(h + 1) * HALF], op0=ALU.add,
                                               op1=ALU.not_equal, accum_out=bad[:, n:n + 1]).then_inc(check_done, 1)

            def norm(q):
                dve.wait_ge(x_in[q], 16)
                if q:
                    dve.wait_ge(mean_ready, q)
                for b in range(LANES):
                    ins = nc.vector.bn_stats(stats[:, b, :], acc[:, LANES * q + b, :])
                step(ins)
                for b in range(LANES):
                    ins = nc.vector.bn_aggr(meanvar[:, LANES * q + b, :], stats[:, b, :])
                ins.then_inc(mean_ready, 1)

            def degrees(u):
                i0, i1 = 2 * u, 2 * u + 2
                dve.wait_ge(cast_done, HALVES * i1)
                step(nc.vector.scalar_tensor_tensor(out=deg[:, i0:i1], in0=rowsum[:, i0:i1, 0], scalar=1.0,
                                                    in1=rowsum[:, i0:i1, 1], op0=ALU.add, op1=ALU.add))
                nc.vector.tensor_scalar(mask[:, i0:i1], deg[:, i0:i1], 0.0, None, ALU.is_gt)
                step(nc.vector.tensor_scalar(zin[:, 0, :], deg[:, i0:i1], DEG_FLOOR, None, ALU.max))
                dve.wait_ge(mean_ready, u // 2 + 1)
                step(nc.vector.scalar_tensor_tensor(out=zin[:, 1, :], in0=meanvar[:, i0:i1, 1], scalar=EPS,
                                                    in1=zin[:, 0, :], op0=ALU.add, op1=ALU.mult))
                nc.vector.reciprocal(zrec[:], zin[:]).then_inc(zrec_ready, 1)

            def high_part(u):
                dve.wait_ge(acc_ready, u + 1)
                nc.vector.tensor_copy(part16(u, 0), pair(u)).then_inc(high_ready, 1)

            sums_at = [0]

            def add_sums():
                k = sums_at[0]
                sums_at[0] += 1
                n = sums[k]
                p = ring_items[n][1]
                dve.wait_ge(sums_made, k + 1)
                dve.wait_ge(g_ready, p + 1)
                if k:
                    dve.wait_ge(sums_added, k)
                nc.vector.tensor_tensor(pair(p), pair(p), ring[:, bank_of[n], :], ALU.add).then_inc(sums_added, 1)
                if last_sum[p] == k:
                    finish(p, k)

            def finish(p, k):
                if p == finish_order[0]:
                    dve.wait_ge(bias_in, 16)
                dve.wait_ge(sums_added, k + 1)
                for i in (2 * p, 2 * p + 1):
                    ins = nc.vector.scalar_tensor_tensor(out=acc[:, i, :], in0=acc[:, i, :],
                                                         scalar=dinv_out[:, i:i + 1], in1=bias_sb[:],
                                                         op0=ALU.mult, op1=ALU.add)
                step(ins)
                step(nc.vector.scalar_tensor_tensor(out=pair(p), in0=pair(p), scalar=SLOPE, in1=pair(p),
                                                    op0=ALU.mult, op1=ALU.max))
                dve.wait_ge(xres_in[p // 2], 16)
                again = x_again(p // 2)[:, 2 * (p % 2):2 * (p % 2) + 2, :].rearrange("p b c -> p (b c)")
                nc.vector.tensor_tensor(pair(p), pair(p), again, ALU.add).then_inc(out_ready, 1)

            check(0, 0)
            norm(0)
            dve.wait_ge(w_in, 32)
            nc.vector.tensor_reduce(scale[:, 0:1], w_sb[:].rearrange("p a k c -> p (a k c)"), AX_X, ALU.max,
                                    apply_absolute_value=True).then_inc(wmax_ready, 1)
            check(0, 1)
            dve.wait_ge(wmax_all, 1)
            step(nc.vector.tensor_scalar(scale[:, 2:3].bitcast(U32), scale[:, 1:2].bitcast(U32), EXP_MASK, None,
                                         ALU.bitwise_and))
            step(nc.vector.tensor_scalar(scale[:, 2:3], scale[:, 2:3], 2.0 ** -60, 2.0 ** 60, ALU.max, ALU.min))
            step(nc.vector.reciprocal(scale[:, 3:4], scale[:, 2:3]))
            step(nc.vector.tensor_scalar(scale[:, 3:4], scale[:, 3:4], 64.0, None, ALU.mult))
            nc.vector.tensor_scalar(scale[:, 4:5], scale[:, 2:3], 1.0 / 64.0, None, ALU.mult).then_inc(scale_ready, 1)

            due, at = {}, 0
            for t, items in enumerate(slots):
                for it in items:
                    if it[0] == "M":
                        at = max(at, t + 1, 2 * it[1] + 3)
                        due.setdefault(at, []).append(it)
            for t in range(TILES + 2):
                makes = [u for u in range(PAIRS) if g_slot(u) == t]
                if makes:
                    degrees(makes[0])
                if 0 < t < TILES:
                    check(t, 0)
                mine = due.get(t, [])
                for _ in mine[:len(mine) // 2]:
                    add_sums()
                for k in range(1, QUADS):
                    if t == h_slot(k) - 1:
                        norm(k)
                if 0 < t < TILES:
                    check(t, 1)
                for u in makes:
                    if u != makes[0]:
                        degrees(u)
                    high_part(u)
                for _ in mine[len(mine) // 2:]:
                    add_sums()
                if t == TILES:
                    dve.wait_ge(check_done, TILES * HALVES)
                    nc.vector.tensor_reduce(verdict[:, 0:1], bad[:], AX_X, ALU.max)
                    step(nc.vector.tensor_reduce(verdict[:, 1:2], deg[:], AX_X, ALU.min))
                    step(nc.vector.tensor_scalar(verdict[:, 1:2], verdict[:, 1:2], 1.0, None, ALU.is_lt))
                    nc.vector.tensor_tensor(verdict[:, 2:3], verdict[:, 0:1], verdict[:, 1:2],
                                            ALU.max).then_inc(verdict_ready, 1)
            while sums_at[0] < len(sums):
                add_sums()
                if sums_at[0] == len(sums) - 2:
                    dve.wait_ge(verdict_all, 1)
                    nc.vector.tensor_scalar(general_flag[:], verdict[:, 3:4], 0.0, None, ALU.is_gt).then_inc(flag_ready, 1)

            dve.wait_ge(flag_ready, 1)
            with dve.If(adj_is_general(dve)):
                nc.vector.tensor_scalar(c_in[:], c_in[:], scale[:, 4:5], None, ALU.mult).then_inc(gen_step, 1)
                nc.vector.tensor_scalar(dinv_out[:], dinv_out[:], scale[:, 3:4], None, ALU.mult).then_inc(gen_step, 1)
                dve.wait_ge(gen_step, 2)
                for w in range(2):
                    with dve.Fori(w * QUADS // 2, (w + 1) * QUADS // 2) as q:
                        for b in range(LANES):
                            i = q * LANES + b
                            dve.wait_ge(gen_x_in, q * (16 * LANES) + 16 * (b + 1))
                            nc.vector.tensor_scalar(gen_relu, gen_x, meanvar[:, bass.ds(i, 1), 0], 0.0,
                                                    ALU.subtract, ALU.max).then_inc(gen_relu_ready, 1)
                            dve.wait_ge(gen_h_turned, i + 1)
                            nc.vector.tensor_copy(gen_hT, ring[:, 0, 0:C]).then_inc(gen_hT_ready, 1)
                            dve.wait_ge(gen_h_made, i + 1)
                            nc.vector.tensor_scalar(gen_g[:, bass.ds(i, 1), :].rearrange("p o c -> p (o c)"),
                                                    ring[:, 1, 0:C], c_in[:, bass.ds(i, 1)], None,
                                                    ALU.mult).then_inc(gen_g_ready, 1)
                with dve.Fori(0, QUADS) as q:
                    for b in range(LANES):
                        i = q * LANES + b
                        for k in range(TILES // 4):
                            dve.wait_ge(gen_turned, i * (TILES // 4) + (k + 1))
                            nc.vector.tensor_copy(gen_adjT[:, k % 2, :], ring[:, k % 2, :]).then_inc(gen_adjT_ready, 1)
                        dve.wait_ge(gen_sum_made, i + 1)
                        dve.wait_ge(gen_adj_in, q * (32 * LANES) + 32 * (b + 1))
                        nc.vector.tensor_tensor(gen_y, gen_g[:, bass.ds(i, 1), :].rearrange("p o c -> p (o c)"),
                                                ring[:, 2, 0:C], ALU.add).then_inc(gen_step, 1)
                        dve.wait_ge(gen_step, i * 3 + 3)
                        nc.vector.scalar_tensor_tensor(out=gen_y, in0=gen_y, scalar=dinv_out[:, bass.ds(i, 1)],
                                                       in1=bias_sb[:], op0=ALU.mult, op1=ALU.add).then_inc(gen_step, 1)
                        dve.wait_ge(gen_step, i * 3 + 4)
                        nc.vector.scalar_tensor_tensor(out=gen_y, in0=gen_y, scalar=SLOPE, in1=gen_y,
                                                       op0=ALU.mult, op1=ALU.max).then_inc(gen_step, 1)
                        dve.wait_ge(gen_step, i * 3 + 5)
                        nc.vector.tensor_tensor(gen_y, gen_y, gen_x, ALU.add).then_inc(gen_y_ready, 1)

        @block.tensor
        def _(pe):
            ring_at = [0]

            def turn_adj(t):
                for bank in range(2):
                    if bank == 0:
                        pe.wait_ge(cast_done, HALVES * t + 1)
                    else:
                        pe.wait_ge(cast_done, HALVES * t + 2)
                    if t:
                        pe.wait_ge(words_ready, 2 * (t - 1) + bank + 1)
                    for k in range(4):
                        J = 4 * bank + k
                        ins = pe.transpose(tr[:, bank, k, :],
                                           adj8[:, t % 2, J * LANES * P:(J + 1) * LANES * P].bitcast(F32), ident[:])
                    ins.then_inc(adj_turned, 1)

            def item(it):
                n = ring_at[0]
                ring_at[0] += 1
                bank = ring[:, bank_of[n], :]
                if n >= RING:
                    who, count = evac_count[n - RING]
                    pe.wait_ge(act_evac if who == "act" else sums_added, count)
                if it[0] == "X":
                    _, q, e = it
                    pe.wait_ge(centred, q + 1)
                    for a in range(2):
                        for k in range(KC):
                            at = (a * KC + k) * P
                            ins = pe.transpose(bank[:, at:at + P], centre[:, 2 * e + a, k * P:(k + 1) * P], ident[:])
                    ins.then_inc(h_turned, 1)
                elif it[0] == "H":
                    _, q, e = it
                    if q == 0:
                        pe.wait_ge(w_in, 32)
                    pe.wait_ge(act_evac, evac_count[ring_items.index(("X", q, e))][1])
                    w = 0 if q < QUADS // 2 else 1
                    for a in range(2):
                        for k in range(KC):
                            ins = pe.matmul(bank[:, a * C:(a + 1) * C], hT[:, e, a, k, :], w_sb[:, w, k, :],
                                            start=(k == 0), stop=(k == KC - 1))
                    ins.then_inc(h_made, 1)
                else:
                    _, p, us = it
                    pe.wait_ge(words_ready, 2 * (2 * p + 1) + 2)
                    pe.wait_ge(g_ready, us[-1] + 1)
                    for a in range(2):
                        for u in us:
                            for b in range(2):
                                for part in range(2):
                                    ins = pe.matmul(bank[:, a * C:(a + 1) * C],
                                                    weights8(2 * p + a, u // 2, 2 * (u % 2) + b),
                                                    part16(u, part)[:, b * C:(b + 1) * C],
                                                    start=(u == us[0] and b == 0 and part == 0),
                                                    stop=(u == us[-1] and b == 1 and part == 1))
                    ins.then_inc(sums_made, 1)

            pe.wait_ge(ident_ready, 1)
            for t, items in enumerate(slots):
                if t < TILES:
                    turn_adj(t)
                for it in items:
                    item(it)
            for it in rest:
                item(it)

            pe.wait_ge(flag_ready, 1)
            with pe.If(adj_is_general(pe)):
                pe.wait_ge(sums_added, len(sums))
                for w in range(2):
                    with pe.Fori(w * QUADS // 2, (w + 1) * QUADS // 2) as q:
                        for b in range(LANES):
                            i = q * LANES + b
                            pe.wait_ge(gen_relu_ready, i + 1)
                            for k in range(KC):
                                ins = pe.transpose(ring[:, 0, k * P:(k + 1) * P], gen_relu[:, k * P:(k + 1) * P],
                                                   ident[:])
                            ins.then_inc(gen_h_turned, 1)
                            pe.wait_ge(gen_hT_ready, i + 1)
                            for k in range(KC):
                                ins = pe.matmul(ring[:, 1, 0:C], gen_hT[:, k * P:(k + 1) * P], w_sb[:, w, k, :],
                                                start=(k == 0), stop=(k == KC - 1))
                            ins.then_inc(gen_h_made, 1)
                pe.wait_ge(gen_g_ready, TILES)
                with pe.Fori(0, QUADS) as q:
                    for b in range(LANES):
                        i = q * LANES + b
                        pe.wait_ge(gen_adj_in, q * (32 * LANES) + 32 * (b + 1))
                        for k in range(TILES // 4 + 1):
                            if k < TILES // 4:
                                if k >= 2:
                                    pe.wait_ge(gen_adjT_ready, i * (TILES // 4) + (k - 1))
                                cols = gen_adj[:, k * 4 * P:(k + 1) * 4 * P].rearrange("p (w j) -> p j w", j=4)
                                for j in range(4):
                                    ins = pe.transpose(ring[:, k % 2, j * P:(j + 1) * P], cols[:, j, :], ident[:])
                                ins.then_inc(gen_turned, 1)
                            if k >= 1:
                                pe.wait_ge(gen_adjT_ready, i * (TILES // 4) + k)
                                for j in range(4):
                                    ins = pe.matmul(ring[:, 2, 0:C], gen_adjT[:, (k - 1) % 2, j * P:(j + 1) * P],
                                                    gen_g[:, 4 * (k - 1) + j, :], start=(k == 1 and j == 0),
                                                    stop=(k == TILES // 4 and j == 3))
                        ins.then_inc(gen_sum_made, 1)


_INS = ["x", "adj", "L0_gnn_weightr", "L0_gnn_weightd", "L0_gnn_bias"]
_OUT = ((4096, 256), "float32")


def kernel(**inputs):
    import numpy as _np
    import concourse.bacc as _bacc
    from concourse import mybir as _mybir
    from concourse.bass_utils import run_bass_kernel_spmd as _run

    nc = _bacc.Bacc("TRN2", target_bir_lowering=False, num_devices=1)
    arrays, args = {}, []
    for name in _INS:
        a = _np.ascontiguousarray(inputs[name])
        arrays[f"in_{name}_dram"] = a
        args.append(nc.dram_tensor(f"in_{name}_dram", a.shape, _mybir.dt.from_np(a.dtype), kind="ExternalInput").ap())
    dt = _mybir.dt.from_np(_np.dtype(_OUT[1]))
    args.append(nc.dram_tensor("out_0_dram", _OUT[0], dt, kind="ExternalOutput").ap())
    gnn_layer(nc, *args)
    r = _run(nc, [arrays], core_ids=[0])
    return r.results[0]["out_0_dram"]
```
